# Optimizing a Trainium2 kernel written in Bass

```python
import numpy as np
import jax
import jax.numpy as jnp

def _softmax(x, axis=-1):
    return jax.nn.softmax(x, axis=axis)

def _gelu(x):
    return jax.nn.gelu(x, approximate=True)

def _silu(x):
    return jax.nn.silu(x)

def _sigmoid(x):
    return jax.nn.sigmoid(x)

def _layernorm(x, axis=-1, eps=1e-05):
    m = jnp.mean(x, axis=axis, keepdims=True)
    v = jnp.var(x, axis=axis, keepdims=True)
    return (x - m) / jnp.sqrt(v + eps)

def _scatter_add(tgt, idx, src, axis=0):
    return tgt.at[idx].add(src)

def _segment_sum(src, seg, n):
    return jax.ops.segment_sum(src, seg, n)
kernel_name = 'mk_dlrm_tower_d1_rec_r8_4334e6'

def setup_inputs(seed: int=0):
    np.random.seed(seed)
    _w = jnp.asarray

    def _rec_inputs():
        import jax
        import jax.numpy as jnp
        _tk = jax.random.key(seed)
        dense_ctx = jax.random.normal(jax.random.fold_in(_tk, 190), (512, 16), jnp.float32)
        ids = jnp.stack([jax.random.randint(jax.random.fold_in(_tk, 200 + f), (512,), 0, v, jnp.int32) for f, v in enumerate([125000, 12500, 12500, 1250, 12500, 1000, 12500, 1250, 1250, 12500, 1000, 12500, 1000, 1250, 12500, 1250, 1250, 1250, 1250, 12500, 1250, 1250, 1250, 1000, 1000, 1000, 1250])], axis=1)
        tbl_0 = 0.05 * jax.random.normal(jax.random.fold_in(_tk, 500 + 0), (125000, 128), jnp.float32)
        tbl_1 = 0.05 * jax.random.normal(jax.random.fold_in(_tk, 500 + 1), (12500, 128), jnp.float32)
        tbl_2 = 0.05 * jax.random.normal(jax.random.fold_in(_tk, 500 + 2), (12500, 128), jnp.float32)
        tbl_3 = 0.05 * jax.random.normal(jax.random.fold_in(_tk, 500 + 3), (1250, 128), jnp.float32)
        tbl_4 = 0.05 * jax.random.normal(jax.random.fold_in(_tk, 500 + 4), (12500, 128), jnp.float32)
        tbl_5 = 0.05 * jax.random.normal(jax.random.fold_in(_tk, 500 + 5), (1000, 128), jnp.float32)
        tbl_6 = 0.05 * jax.random.normal(jax.random.fold_in(_tk, 500 + 6), (12500, 128), jnp.float32)
        tbl_7 = 0.05 * jax.random.normal(jax.random.fold_in(_tk, 500 + 7), (1250, 128), jnp.float32)
        tbl_8 = 0.05 * jax.random.normal(jax.random.fold_in(_tk, 500 + 8), (1250, 128), jnp.float32)
        tbl_9 = 0.05 * jax.random.normal(jax.random.fold_in(_tk, 500 + 9), (12500, 128), jnp.float32)
        tbl_10 = 0.05 * jax.random.normal(jax.random.fold_in(_tk, 500 + 10), (1000, 128), jnp.float32)
        tbl_11 = 0.05 * jax.random.normal(jax.random.fold_in(_tk, 500 + 11), (12500, 128), jnp.float32)
        tbl_12 = 0.05 * jax.random.normal(jax.random.fold_in(_tk, 500 + 12), (1000, 128), jnp.float32)
        tbl_13 = 0.05 * jax.random.normal(jax.random.fold_in(_tk, 500 + 13), (1250, 128), jnp.float32)
        tbl_14 = 0.05 * jax.random.normal(jax.random.fold_in(_tk, 500 + 14), (12500, 128), jnp.float32)
        tbl_15 = 0.05 * jax.random.normal(jax.random.fold_in(_tk, 500 + 15), (1250, 128), jnp.float32)
        tbl_16 = 0.05 * jax.random.normal(jax.random.fold_in(_tk, 500 + 16), (1250, 128), jnp.float32)
        tbl_17 = 0.05 * jax.random.normal(jax.random.fold_in(_tk, 500 + 17), (1250, 128), jnp.float32)
        tbl_18 = 0.05 * jax.random.normal(jax.random.fold_in(_tk, 500 + 18), (1250, 128), jnp.float32)
        tbl_19 = 0.05 * jax.random.normal(jax.random.fold_in(_tk, 500 + 19), (12500, 128), jnp.float32)
        tbl_20 = 0.05 * jax.random.normal(jax.random.fold_in(_tk, 500 + 20), (1250, 128), jnp.float32)
        tbl_21 = 0.05 * jax.random.normal(jax.random.fold_in(_tk, 500 + 21), (1250, 128), jnp.float32)
        tbl_22 = 0.05 * jax.random.normal(jax.random.fold_in(_tk, 500 + 22), (1250, 128), jnp.float32)
        tbl_23 = 0.05 * jax.random.normal(jax.random.fold_in(_tk, 500 + 23), (1000, 128), jnp.float32)
        tbl_24 = 0.05 * jax.random.normal(jax.random.fold_in(_tk, 500 + 24), (1000, 128), jnp.float32)
        tbl_25 = 0.05 * jax.random.normal(jax.random.fold_in(_tk, 500 + 25), (1000, 128), jnp.float32)
        tbl_26 = 0.05 * jax.random.normal(jax.random.fold_in(_tk, 500 + 26), (1250, 128), jnp.float32)
        _rk = jax.random.fold_in(_tk, 7)
        W_top1 = 0.0521996 * jax.random.normal(jax.random.fold_in(_tk, 801), (367, 512), jnp.float32)
        W_top2 = 0.0441942 * jax.random.normal(jax.random.fold_in(_tk, 802), (512, 256), jnp.float32)
        W_top3 = 0.0625 * jax.random.normal(jax.random.fold_in(_tk, 803), (256, 1), jnp.float32)
        b_top1 = jnp.zeros((512,), jnp.float32)
        b_top2 = jnp.zeros((256,), jnp.float32)
        return (dense_ctx, ids, tbl_0, tbl_1, tbl_2, tbl_3, tbl_4, tbl_5, tbl_6, tbl_7, tbl_8, tbl_9, tbl_10, tbl_11, tbl_12, tbl_13, tbl_14, tbl_15, tbl_16, tbl_17, tbl_18, tbl_19, tbl_20, tbl_21, tbl_22, tbl_23, tbl_24, tbl_25, tbl_26, W_top1, b_top1, W_top2, b_top2, W_top3)
    dense_ctx, ids, tbl_0, tbl_1, tbl_2, tbl_3, tbl_4, tbl_5, tbl_6, tbl_7, tbl_8, tbl_9, tbl_10, tbl_11, tbl_12, tbl_13, tbl_14, tbl_15, tbl_16, tbl_17, tbl_18, tbl_19, tbl_20, tbl_21, tbl_22, tbl_23, tbl_24, tbl_25, tbl_26, W_top1, b_top1, W_top2, b_top2, W_top3 = _rec_inputs()

    def _L0_rec_setup():
        import jax, jax.numpy as jnp
        import numpy as np
        NUM_FEATURES = 27
        EMBED_DIM = 128
        BATCH = 4096
        key = jax.random.key(seed)
        inputs = jax.random.normal(key, (BATCH, NUM_FEATURES, EMBED_DIM), dtype=jnp.float32)
        return {'inputs': inputs}
    _L0_rec_all = _L0_rec_setup()
    _L0_rec_in = {k: v for k, v in _L0_rec_all.items() if k in ()}
    del _L0_rec_all
    return {'dense_ctx': dense_ctx, 'ids': ids, 'tbl_0': tbl_0, 'tbl_1': tbl_1, 'tbl_2': tbl_2, 'tbl_3': tbl_3, 'tbl_4': tbl_4, 'tbl_5': tbl_5, 'tbl_6': tbl_6, 'tbl_7': tbl_7, 'tbl_8': tbl_8, 'tbl_9': tbl_9, 'tbl_10': tbl_10, 'tbl_11': tbl_11, 'tbl_12': tbl_12, 'tbl_13': tbl_13, 'tbl_14': tbl_14, 'tbl_15': tbl_15, 'tbl_16': tbl_16, 'tbl_17': tbl_17, 'tbl_18': tbl_18, 'tbl_19': tbl_19, 'tbl_20': tbl_20, 'tbl_21': tbl_21, 'tbl_22': tbl_22, 'tbl_23': tbl_23, 'tbl_24': tbl_24, 'tbl_25': tbl_25, 'tbl_26': tbl_26, 'W_top1': W_top1, 'b_top1': b_top1, 'W_top2': W_top2, 'b_top2': b_top2, 'W_top3': W_top3}

def reference(dense_ctx, ids, tbl_0, tbl_1, tbl_2, tbl_3, tbl_4, tbl_5, tbl_6, tbl_7, tbl_8, tbl_9, tbl_10, tbl_11, tbl_12, tbl_13, tbl_14, tbl_15, tbl_16, tbl_17, tbl_18, tbl_19, tbl_20, tbl_21, tbl_22, tbl_23, tbl_24, tbl_25, tbl_26, W_top1, b_top1, W_top2, b_top2, W_top3):
    import jax
    import jax.numpy as jnp

    def _L0_rec_ref(inputs):
        import jax, jax.numpy as jnp
        import numpy as np
        NUM_FEATURES = 27
        EMBED_DIM = 128
        BATCH = 4096
        interactions = jnp.einsum('bnd,bmd->bnm', inputs, inputs)
        n = inputs.shape[1]
        i, j = jnp.triu_indices(n, k=1)
        return interactions[:, i, j]
    e = jnp.stack([tbl_0[ids[:, 0]], tbl_1[ids[:, 1]], tbl_2[ids[:, 2]], tbl_3[ids[:, 3]], tbl_4[ids[:, 4]], tbl_5[ids[:, 5]], tbl_6[ids[:, 6]], tbl_7[ids[:, 7]], tbl_8[ids[:, 8]], tbl_9[ids[:, 9]], tbl_10[ids[:, 10]], tbl_11[ids[:, 11]], tbl_12[ids[:, 12]], tbl_13[ids[:, 13]], tbl_14[ids[:, 14]], tbl_15[ids[:, 15]], tbl_16[ids[:, 16]], tbl_17[ids[:, 17]], tbl_18[ids[:, 18]], tbl_19[ids[:, 19]], tbl_20[ids[:, 20]], tbl_21[ids[:, 21]], tbl_22[ids[:, 22]], tbl_23[ids[:, 23]], tbl_24[ids[:, 24]], tbl_25[ids[:, 25]], tbl_26[ids[:, 26]]], axis=1)
    z = _L0_rec_ref(e)
    z = z.reshape(z.shape[0], -1)
    h = jnp.concatenate([z, dense_ctx], axis=1)
    h = jnp.maximum(h @ W_top1 + b_top1, 0.0)
    h = jnp.maximum(h @ W_top2 + b_top2, 0.0)
    y = h @ W_top3
    return y

_drawn_inputs = setup_inputs


def setup_inputs(seed=0):
    import zlib

    import numpy as np

    out = dict(_drawn_inputs(seed))
    spreads = {'b_top1': (0.0, 0.1), 'b_top2': (0.0, 0.1)}
    factors = {}
    for name, (base, spread) in spreads.items():
        noise = np.random.default_rng([zlib.crc32(name.encode()), seed]).standard_normal(out[name].shape)
        drawn = base * np.exp(spread * noise) if base else spread * noise
        out[name] = jnp.asarray(drawn.astype(out[name].dtype))
    for name, factor in factors.items():
        out[name] = (out[name] * factor).astype(out[name].dtype)
    return out
```

```python
import concourse.bass as bass
from concourse import mybir
from contextlib import ExitStack


def dlrm_tower(nc, dense_rows, ids, tables, w1_rows, b1_cols, w2, b2_cols, w3_cols, out):
    fp32 = mybir.dt.float32
    ALU = mybir.AluOpType
    ACT = mybir.ActivationFunctionType

    P = 128
    B, F = ids.shape
    D = tables[0].shape[1]
    T = B // P
    S = 4
    G = P // S
    Q = 32
    SF = S * F
    QUADS = [list(range(f, min(f + 4, F))) for f in range(0, F, 4)]
    NQ = len(QUADS)
    EARLY = 3
    GB = 4
    GU = 2 * GB
    U = G // GU
    K = (F - 1) // 2
    J = F + K
    I = 9
    NC = F // I
    PAIRS = I * K
    DN = dense_rows.shape[0]
    DENSE = [(0, P - PAIRS), (P - PAIRS, DN), (DN, DN)]
    ROWS = [PAIRS + b - a for a, b in DENSE]
    N1 = w2.shape[0] // P
    N2 = w2.shape[1] // P

    ctx = ExitStack()
    with ctx:
        def sb(name, shape, dt=fp32):
            return ctx.enter_context(nc.sbuf_tensor(name, shape, dt))

        def pb(name, shape, dt=fp32):
            return ctx.enter_context(nc.psum_tensor(name, shape, dt))

        def sem(name):
            return ctx.enter_context(nc.semaphore(name))

        ids_sb = sb("ids_sb", [P, T, F], mybir.dt.int32)
        ident = sb("ident", [P, P])
        rows = sb("rows", [P, T, F, D])
        ET = sb("ET", [P, T, G, S, Q])
        gram = sb("gram", [P, 2, F, G])
        zT = sb("zT", [P, T, NC, P])
        w1_sb = sb("w1_sb", [P, NC, N1 * P])
        w2_sb = sb("w2_sb", [P, N1, N2 * P])
        w3_sb = sb("w3_sb", [P, N2])
        b1_sb = sb("b1_sb", [P, N1])
        b2_sb = sb("b2_sb", [P, N2])
        h1 = sb("h1", [P, N1, P])
        h2 = sb("h2", [P, N2, P])
        y_sb = sb("y_sb", [1, B])

        psT = pb("psT", [P, 2, 4, P])
        psG = pb("psG", [P, 2, 2, 512])
        psH = pb("psH", [P, 2, 4, P])
        psY = psH[0:1, 0, 3, :]

        scratch = nc.dram_tensor("pairs_scratch", (T, P, J, G), fp32, kind="Internal").ap()

        ids_in = sem("ids_in")
        ident_zero = sem("ident_zero")
        ident_ready = sem("ident_ready")
        pad_zero = sem("pad_zero")
        w1_in = sem("w1_in")
        w2_in = sem("w2_in")
        small_in = sem("small_in")
        dense_in = sem("dense_in")
        gathered = [[sem(f"gathered_{t}_{q}") for q in range(NQ)] for t in range(T)]
        transposed = sem("transposed")
        et_dve = sem("et_dve")
        et_act = sem("et_act")
        multiplied = sem("multiplied")
        gram_dve = sem("gram_dve")
        gram_act = sem("gram_act")
        scratch_in = [sem(f"scratch_in_{t}") for t in range(T)]
        z_in = [sem(f"z_in_{t}") for t in range(T)]
        l1_done = sem("l1_done")
        l2_done = sem("l2_done")
        l3_done = sem("l3_done")
        h1_dve = sem("h1_dve")
        h1_act = sem("h1_act")
        h2_dve = sem("h2_dve")
        h2_act = sem("h2_act")
        y_ready = sem("y_ready")
        out_done = sem("out_done")

        def quad_no(t, q):
            return t * NQ + q

        def dve_quads(n):
            return (n + 1) // 2

        def act_quads(n):
            return n // 2

        def quad_view(t, q):
            fs = QUADS[q]
            n = quad_no(t, q)
            src = psT[:, n % 2, 0:len(fs), :].rearrange("d f (s g) -> d g s f", s=S)
            return ET[:, t, :, :, fs[0]:fs[-1] + 1], src

        def gram_view(t, u, s):
            m = t * U + u
            src = psG[Q * s:Q * (s + 1), m % 2, :, 0:GB * SF].rearrange(
                "i b (g c) -> i b g c", c=SF)[:, :, :, F * s:F * (s + 1)]
            dst = gram[Q * s:Q * (s + 1), t % 2, :, GU * u:GU * (u + 1)].rearrange(
                "i j (b g) -> i b g j", b=2)
            return dst, src

        block = ctx.enter_context(nc.Block())

        @block.sync
        def _(sp):
            sp.dma_start(ids_sb[:, :, :], ids.rearrange("(t p) f -> p t f", p=P)).then_inc(ids_in, 16)
            for c in range(NC):
                sp.dma_start(w1_sb[0:ROWS[c], c, :], w1_rows[sum(ROWS[:c]):sum(ROWS[:c + 1]), :]).then_inc(w1_in, 16)
            for c, (a, b) in enumerate(DENSE):
                if b > a:
                    sp.dma_start(zT[PAIRS:PAIRS + b - a, :, c, :],
                                 dense_rows[a:b, :].rearrange("k (t p) -> k t p", p=P)).then_inc(dense_in, 16)
            sp.dma_start(w2_sb[:, :, :], w2.rearrange("(k p) n -> p k n", p=P)).then_inc(w2_in, 16)
            sp.dma_start(b1_sb[:, :], b1_cols).then_inc(small_in, 16)
            sp.dma_start(b2_sb[:, :], b2_cols).then_inc(small_in, 16)
            sp.dma_start(w3_sb[:, :], w3_cols).then_inc(small_in, 16)
            for t in range(T):
                sp.wait_ge(gram_dve, U * (t + 1))
                sp.wait_ge(gram_act, U * (t + 1))
                sp.dma_start(scratch[t, :, 0:F, :], gram[:, t % 2, :, :]).then_inc(scratch_in[t], 16)
                sp.dma_start(scratch[t, :, F:J, :], gram[:, t % 2, 0:K, :]).then_inc(scratch_in[t], 16)
                sp.wait_ge(scratch_in[t], 32)
                for c in range(NC):
                    for s in range(S):
                        first = scratch[t, Q * s + I * c, I * c + 1:I * c + 2, :]
                        src = bass.AP(first.tensor, first.offset, [[(J + 1) * G, I], [G, K], [1, G]])
                        sp.dma_start(zT[0:PAIRS, t, c, G * s:G * (s + 1)], src).then_inc(z_in[t], 16)
            sp.wait_ge(y_ready, T)
            sp.dma_start(out.rearrange("b o -> o b"), y_sb[:, :]).then_inc(out_done, 16)
            sp.wait_ge(out_done, 16)

        @block.gpsimd
        def _(pool):
            pool.memset(ident[:, :], 0.0).then_inc(ident_zero, 1)
            pool.wait_ge(ident_zero, 1)
            pool.affine_select(out=ident[:, :], in_=ident[:, :], compare_op=ALU.not_equal, fill=1.0, base=0,
                               pattern=[[-1, P]], channel_multiplier=1).then_inc(ident_ready, 1)
            pool.wait_ge(ids_in, 16)
            for t in range(T):
                for q in range(NQ):
                    for f in QUADS[q]:
                        pool.indirect_dma_start(
                            out=rows[:, t, f, :], out_offset=None, in_=tables[f],
                            in_offset=bass.IndirectOffsetOnAxis(ap=ids_sb[:, t, f:f + 1], axis=0),
                        ).then_inc(gathered[t][q], 16)

        @block.tensor
        def _(pe):
            def transposes(t, q):
                n = quad_no(t, q)
                pe.wait_ge(gathered[t][q], 16 * len(QUADS[q]))
                if n >= 2:
                    if n % 2 == 0:
                        pe.wait_ge(et_dve, dve_quads(n - 1))
                    else:
                        pe.wait_ge(et_act, act_quads(n - 1))
                for x, f in enumerate(QUADS[q]):
                    last = pe.transpose(psT[:, n % 2, x, :], rows[:, t, f, :], ident[:, :])
                last.then_inc(transposed, 1)

            def products(t):
                n = quad_no(t + 1, 0)
                pe.wait_ge(et_dve, dve_quads(n))
                pe.wait_ge(et_act, act_quads(n))
                for u in range(U):
                    m = t * U + u
                    if m >= 2:
                        pe.wait_ge(gram_dve, m - 1)
                        pe.wait_ge(gram_act, m - 1)
                    for x in range(GU):
                        group = ET[:, t, GU * u + x, :, :]
                        o = psG[:, m % 2, x // GB, SF * (x % GB):SF * (x % GB + 1)]
                        last = pe.matmul(o, group.rearrange("d s f -> d (s f)"), group[:, :, 0:F], start=True, stop=True)
                    last.then_inc(multiplied, 1)

            def mlp(t):
                pe.wait_ge(z_in[t], 16 * NC * S)
                if t == 0:
                    pe.wait_ge(w1_in, 16 * NC)
                    pe.wait_ge(dense_in, 32)
                else:
                    pe.wait_ge(y_ready, t)
                    pe.wait_ge(h2_act, t)
                for n in range(N1):
                    for c in range(NC):
                        last = pe.matmul(psH[:, n // 2, n % 2, :], w1_sb[0:ROWS[c], c, P * n:P * (n + 1)],
                                         zT[0:ROWS[c], t, c, :], start=c == 0, stop=c == NC - 1)
                    if n % 2 == 1:
                        last.then_inc(l1_done, 1)
                if t == 0:
                    pe.wait_ge(w2_in, 16)
                    pe.wait_ge(small_in, 48)
                pe.wait_ge(h1_dve, 2 * (t + 1))
                pe.wait_ge(h1_act, 2 * (t + 1))
                for n in range(N2):
                    for k in range(N1):
                        last = pe.matmul(psH[:, n, 2, :], w2_sb[:, k, P * n:P * (n + 1)], h1[:, k, :],
                                         start=k == 0, stop=k == N1 - 1)
                    last.then_inc(l2_done, 1)
                pe.wait_ge(h2_dve, t + 1)
                pe.wait_ge(h2_act, t + 1)
                for k in range(N2):
                    last = pe.matmul(psY, w3_sb[:, k:k + 1], h2[:, k, :], start=k == 0, stop=k == N2 - 1)
                last.then_inc(l3_done, 1)

            pe.wait_ge(ident_ready, 1)
            pe.wait_ge(pad_zero, 1)
            for t in range(T):
                for q in range(NQ):
                    if t >= 1 and q == EARLY:
                        mlp(t - 1)
                    transposes(t, q)
                products(t)
            mlp(T - 1)

        @block.vector
        def _(dve):
            def quad_copy(t, q):
                n = quad_no(t, q)
                if n % 2 == 0:
                    dve.wait_ge(transposed, n + 1)
                    dve.tensor_copy(*quad_view(t, q)).then_inc(et_dve, 1)

            def gram_copies(t):
                if t >= 2:
                    dve.wait_ge(scratch_in[t - 2], 32)
                for u in range(U):
                    dve.wait_ge(multiplied, t * U + u + 1)
                    dve.tensor_copy(*gram_view(t, u, 0))
                    dve.tensor_copy(*gram_view(t, u, 1)).then_inc(gram_dve, 1)

            def relus(t):
                dve.wait_ge(l1_done, 2 * t + 1)
                for n in range(2):
                    dve.tensor_scalar(h1[:, n, :], psH[:, 0, n, :], b1_sb[:, n:n + 1], 0.0, ALU.add, ALU.max
                                      ).then_inc(h1_dve, 1)
                dve.wait_ge(l2_done, N2 * t + 1)
                dve.tensor_scalar(h2[:, 0, :], psH[:, 0, 2, :], b2_sb[:, 0:1], 0.0, ALU.add, ALU.max
                                  ).then_inc(h2_dve, 1)
                dve.wait_ge(l3_done, t + 1)
                dve.tensor_copy(y_sb[:, P * t:P * (t + 1)], psY).then_inc(y_ready, 1)

            dve.memset(ET[:, :, :, :, F:Q].rearrange("d t g s f -> d (t g s) f"), 0.0).then_inc(pad_zero, 1)
            dve.wait_ge(small_in, 48)
            for t in range(T):
                for q in range(NQ):
                    if t >= 1 and q == EARLY:
                        relus(t - 1)
                    quad_copy(t, q)
                gram_copies(t)
            relus(T - 1)

        @block.scalar
        def _(act):
            def quad_copy(t, q):
                n = quad_no(t, q)
                if n % 2 == 1:
                    act.wait_ge(transposed, n + 1)
                    act.copy(*quad_view(t, q)).then_inc(et_act, 1)

            def gram_copies(t):
                if t >= 2:
                    act.wait_ge(scratch_in[t - 2], 32)
                for u in range(U):
                    act.wait_ge(multiplied, t * U + u + 1)
                    act.copy(*gram_view(t, u, 2))
                    act.copy(*gram_view(t, u, 3)).then_inc(gram_act, 1)

            def relus(t):
                act.wait_ge(l1_done, 2 * t + 2)
                for n in range(2, 4):
                    act.activation(h1[:, n, :], psH[:, 1, n - 2, :], ACT.Relu, bias=b1_sb[:, n:n + 1]
                                   ).then_inc(h1_act, 1)
                act.wait_ge(l2_done, N2 * (t + 1))
                act.activation(h2[:, 1, :], psH[:, 1, 2, :], ACT.Relu, bias=b2_sb[:, 1:2]).then_inc(h2_act, 1)

            act.wait_ge(small_in, 48)
            for t in range(T):
                for q in range(NQ):
                    if t >= 1 and q == EARLY:
                        relus(t - 1)
                    quad_copy(t, q)
                gram_copies(t)
            relus(T - 1)


def pair_rows(n_features, n_dense):
    half, each = (n_features - 1) // 2, n_features // 3
    base = n_features * (n_features - 1) // 2
    order, dense = [], 0
    for c in range(3):
        for i in range(each * c, each * (c + 1)):
            for k in range(1, half + 1):
                a, b = sorted((i, (i + k) % n_features))
                order.append(a * n_features - a * (a + 1) // 2 + b - a - 1)
        more = min(n_dense - dense, 128 - each * half)
        order += [base + dense + x for x in range(more)]
        dense += more
    return order


def kernel(**inputs):
    import numpy as np
    import concourse.bacc as bacc
    from concourse.bass_utils import run_bass_kernel_spmd

    def columns(v):
        return np.ascontiguousarray(np.asarray(v).reshape(-1, 128).T)

    ids = np.ascontiguousarray(inputs["ids"])
    n_features = ids.shape[1]
    n_dense = inputs["dense_ctx"].shape[1]
    arrays = {
        "in_dense": np.ascontiguousarray(np.asarray(inputs["dense_ctx"]).T),
        "in_ids": ids,
        "in_w1": np.ascontiguousarray(np.asarray(inputs["W_top1"])[pair_rows(n_features, n_dense)]),
        "in_b1": columns(inputs["b_top1"]),
        "in_w2": np.ascontiguousarray(inputs["W_top2"]),
        "in_b2": columns(inputs["b_top2"]),
        "in_w3": columns(inputs["W_top3"]),
    }
    for f in range(n_features):
        arrays[f"in_tbl_{f}"] = np.ascontiguousarray(inputs[f"tbl_{f}"])

    nc = bacc.Bacc("TRN2", target_bir_lowering=False, num_devices=1)
    aps = {name: nc.dram_tensor(name, a.shape, mybir.dt.from_np(a.dtype), kind="ExternalInput").ap()
           for name, a in arrays.items()}
    out = nc.dram_tensor("out_y", (ids.shape[0], 1), mybir.dt.float32, kind="ExternalOutput").ap()
    dlrm_tower(nc, aps["in_dense"], aps["in_ids"], [aps[f"in_tbl_{f}"] for f in range(n_features)],
               aps["in_w1"], aps["in_b1"], aps["in_w2"], aps["in_b2"], aps["in_w3"], out)
    r = run_bass_kernel_spmd(nc, [arrays], core_ids=[0])
    return r.results[0]["out_y"]
```

```python
import concourse.bass as bass
from concourse import mybir
from contextlib import ExitStack


def dlrm_tower(nc, dense_rows, ids, picked_ids, tables, w1_rows, b1_cols, w2, b2_cols, w3_cols, out):
    fp32 = mybir.dt.float32
    ALU = mybir.AluOpType
    ACT = mybir.ActivationFunctionType

    P = 128
    bf16 = mybir.dt.bfloat16
    fp16 = mybir.dt.float16
    i32 = mybir.dt.int32
    B, FG = ids.shape
    FP = picked_ids.shape[0]
    F = FG + FP
    D = tables[0].shape[1]
    T = B // P
    S = 4
    G = P // S
    Q = 32
    SF = S * F
    QUADS = [list(range(f, min(f + 4, FG))) for f in range(0, FG, 4)]
    NQ = len(QUADS)
    V = 125
    CH = [tables[f].shape[0] // V for f in range(FG, F)]
    CM = max(CH)
    GB = 4
    GU = 2 * GB
    U = G // GU
    K = (F - 1) // 2
    J = F + K
    I = 9
    NC = F // I
    PAIRS = I * K
    DN = dense_rows.shape[0]
    DENSE = [(0, P - PAIRS), (P - PAIRS, DN), (DN, DN)]
    ROWS = [PAIRS + b - a for a, b in DENSE]
    N1 = w2.shape[0] // P
    N2 = w2.shape[1] // P

    ctx = ExitStack()
    with ctx:
        def sb(name, shape, dt=fp32):
            return ctx.enter_context(nc.sbuf_tensor(name, shape, dt))

        def pb(name, shape, dt=fp32):
            return ctx.enter_context(nc.psum_tensor(name, shape, dt))

        def sem(name):
            return ctx.enter_context(nc.semaphore(name))

        ids_sb = sb("ids_sb", [P, T, FG], i32)
        pick_ids = sb("pick_ids", [V, FP, B], i32)
        pick_half = sb("pick_half", [V, 2, B], fp16)
        row_int = sb("row_int", [V, 2, CM], i32)
        row_no = sb("row_no", [V, 2, CM])
        table = sb("table", [V, 2, CM, D])
        parts = sb("parts", [V, 2, 3, CM, D], bf16)
        hot = sb("hot", [V, 2, CM, B], bf16)
        ident = sb("ident", [P, P])
        rows = sb("rows", [P, 2, FG, D])
        ET = sb("ET", [P, T, G, S, Q])
        gram = sb("gram", [P, 2, F, G])
        zT = sb("zT", [P, T, NC, P])
        w1_sb = sb("w1_sb", [P, NC, N1 * P])
        w2_sb = sb("w2_sb", [P, N1, N2 * P])
        w3_sb = sb("w3_sb", [P, N2])
        b1_sb = sb("b1_sb", [P, N1])
        b2_sb = sb("b2_sb", [P, N2])
        h1 = sb("h1", [P, N1, P])
        h2 = sb("h2", [P, N2, P])
        y_sb = sb("y_sb", [1, B])

        psT = pb("psT", [P, 2, 4, P])
        psG = pb("psG", [P, 2, 2, 512])
        psH = pb("psH", [P, 2, 4, P])
        psY = psH[0:1, 0, 3, :]

        scratch = nc.dram_tensor("pairs_scratch", (T, P, J, G), fp32, kind="Internal").ap()

        ids_in = sem("ids_in")
        ident_zero = sem("ident_zero")
        ident_ready = sem("ident_ready")
        pad_zero = sem("pad_zero")
        w1_in = sem("w1_in")
        w2_in = sem("w2_in")
        small_in = sem("small_in")
        dense_in = sem("dense_in")
        gathered = [[sem(f"gathered_{t}_{q}") for q in range(NQ)] for t in range(T)]
        pick_ids_in = sem("pick_ids_in")
        row_int_ready = sem("row_int_ready")
        row_no_ready = sem("row_no_ready")
        table_in = [sem(f"table_in_{k}") for k in range(FP)]
        half_ready = sem("half_ready")
        hot_ready = sem("hot_ready")
        high_ready = sem("high_ready")
        rest_ready = sem("rest_ready")
        middle_ready = sem("middle_ready")
        low_ready = sem("low_ready")
        filled = sem("filled")
        et_dve = sem("et_dve")
        et_act = sem("et_act")
        multiplied = sem("multiplied")
        gram_dve = sem("gram_dve")
        gram_act = sem("gram_act")
        scratch_in = [sem(f"scratch_in_{t}") for t in range(T)]
        z_in = [sem(f"z_in_{t}") for t in range(T)]
        z_last_in = sem("z_last_in")
        l1_done = sem("l1_done")
        l2_done = sem("l2_done")
        l3_done = sem("l3_done")
        h1_dve = sem("h1_dve")
        h1_act = sem("h1_act")
        h2_dve = sem("h2_dve")
        h2_act = sem("h2_act")
        y_ready = sem("y_ready")
        out_done = sem("out_done")

        fills = []
        for q in range(max(FP, NQ)):
            fills += [("pick", k, None) for k in range(q, min(q + 1, FP))]
            fills += [("quad", 0, x) for x in range(q, min(q + 1, NQ))]
        FIRST = len(fills)
        fills += [("quad", t, q) for t in range(1, T) for q in range(NQ)]
        BY_DVE = [n >= FIRST and n % 2 == 0 for n in range(len(fills))]

        def wait_copied(eng, n):
            if sum(BY_DVE[:n]):
                eng.wait_ge(et_dve, sum(BY_DVE[:n]))
            if n - sum(BY_DVE[:n]):
                eng.wait_ge(et_act, n - sum(BY_DVE[:n]))

        def ring_views(n):
            kind, t, q = fills[n]
            if kind == "pick":
                return (ET[:, :, :, :, FG + t],
                        psT[:, n % 2, :, :].rearrange("d t (s g) -> d t g s", s=S))
            fs = QUADS[q]
            return (ET[:, t, :, :, fs[0]:fs[-1] + 1],
                    psT[:, n % 2, 0:len(fs), :].rearrange("d f (s g) -> d g s f", s=S))

        def gram_view(t, u, s):
            m = t * U + u
            src = psG[Q * s:Q * (s + 1), m % 2, :, 0:GB * SF].rearrange(
                "i b (g c) -> i b g c", c=SF)[:, :, :, F * s:F * (s + 1)]
            dst = gram[Q * s:Q * (s + 1), t % 2, :, GU * u:GU * (u + 1)].rearrange(
                "i j (b g) -> i b g j", b=2)
            return dst, src

        def read_pairs(eng, t, c, landed):
            for s in range(S):
                first = scratch[t, Q * s + I * c, I * c + 1:I * c + 2, :]
                src = bass.AP(first.tensor, first.offset, [[(J + 1) * G, I], [G, K], [1, G]])
                eng.dma_start(zT[0:PAIRS, t, c, G * s:G * (s + 1)], src).then_inc(landed, 16)

        block = ctx.enter_context(nc.Block())

        @block.sync
        def _(sp):
            sp.dma_start(ids_sb[:, :, :], ids.rearrange("(t p) f -> p t f", p=P)).then_inc(ids_in, 16)
            for k in range(FP):
                if k >= 2:
                    sp.wait_ge(low_ready, k - 1)
                sp.dma_start(table[:, k % 2, 0:CH[k], :],
                             tables[FG + k].rearrange("(p c) d -> p c d", c=CH[k])).then_inc(table_in[k], 16)
            for c in range(NC):
                sp.dma_start(w1_sb[0:ROWS[c], c, :], w1_rows[sum(ROWS[:c]):sum(ROWS[:c + 1]), :]).then_inc(w1_in, 16)
            for c, (a, b) in enumerate(DENSE):
                if b > a:
                    sp.dma_start(zT[PAIRS:PAIRS + b - a, :, c, :],
                                 dense_rows[a:b, :].rearrange("k (t p) -> k t p", p=P)).then_inc(dense_in, 16)
            sp.dma_start(w2_sb[:, :, :], w2.rearrange("(k p) n -> p k n", p=P)).then_inc(w2_in, 16)
            sp.dma_start(b1_sb[:, :], b1_cols).then_inc(small_in, 16)
            sp.dma_start(b2_sb[:, :], b2_cols).then_inc(small_in, 16)
            sp.dma_start(w3_sb[:, :], w3_cols).then_inc(small_in, 16)
            for t in range(T):
                sp.wait_ge(gram_dve, U * (t + 1))
                sp.wait_ge(gram_act, U * (t + 1))
                sp.dma_start(scratch[t, :, 0:F, :], gram[:, t % 2, :, :]).then_inc(scratch_in[t], 16)
                sp.dma_start(scratch[t, :, F:J, :], gram[:, t % 2, 0:K, :]).then_inc(scratch_in[t], 16)
                sp.wait_ge(scratch_in[t], 32)
                for c in range(NC - 1 if t == T - 1 else NC):
                    read_pairs(sp, t, c, z_in[t])
            sp.wait_ge(y_ready, T)
            sp.dma_start(out.rearrange("b o -> o b"), y_sb[:, :]).then_inc(out_done, 16)
            sp.wait_ge(out_done, 16)

        @block.gpsimd
        def _(pool):
            pool.memset(ident[:, :], 0.0).then_inc(ident_zero, 1)
            pool.wait_ge(ident_zero, 1)
            pool.affine_select(out=ident[:, :], in_=ident[:, :], compare_op=ALU.not_equal, fill=1.0, base=0,
                               pattern=[[-1, P]], channel_multiplier=1).then_inc(ident_ready, 1)
            pool.iota(row_int[:, 0, :], pattern=[[1, CM]], base=0, channel_multiplier=min(CH)).then_inc(row_int_ready, 1)
            pool.iota(row_int[:, 1, :], pattern=[[1, CM]], base=0, channel_multiplier=max(CH)).then_inc(row_int_ready, 1)
            pool.wait_ge(ids_in, 16)
            for t in range(T):
                if t >= 2:
                    pool.wait_ge(filled, fills.index(("quad", t - 2, NQ - 1)) + 1)
                for q in range(NQ):
                    for f in QUADS[q]:
                        pool.indirect_dma_start(
                            out=rows[:, t % 2, f, :], out_offset=None, in_=tables[f],
                            in_offset=bass.IndirectOffsetOnAxis(ap=ids_sb[:, t, f:f + 1], axis=0),
                        ).then_inc(gathered[t][q], 16)
            pool.wait_ge(scratch_in[T - 1], 32)
            read_pairs(pool, T - 1, NC - 1, z_last_in)

        @block.tensor
        def _(pe):
            def transposes(n):
                _, t, q = fills[n]
                pe.wait_ge(gathered[t][q], 16 * len(QUADS[q]))
                if n >= 2:
                    wait_copied(pe, n - 1)
                for x, f in enumerate(QUADS[q]):
                    last = pe.transpose(psT[:, n % 2, x, :], rows[:, t % 2, f, :], ident[:, :])
                last.then_inc(filled, 1)

            def pick(n):
                k = fills[n][1]
                if n >= 2:
                    wait_copied(pe, n - 1)
                pe.wait_ge(hot_ready, k + 1)
                for x, ready in enumerate((high_ready, middle_ready, low_ready)):
                    pe.wait_ge(ready, k + 1)
                    for c in range(CH[k]):
                        last = pe.matmul(psT[:, n % 2, :, :].rearrange("d t p -> d (t p)"),
                                         parts[:, k % 2, x, c, :], hot[:, k % 2, c, :],
                                         start=x == 0 and c == 0, stop=x == 2 and c == CH[k] - 1)
                last.then_inc(filled, 1)

            def products(t):
                wait_copied(pe, FIRST + NQ * t)
                for u in range(U):
                    m = t * U + u
                    if m >= 2:
                        pe.wait_ge(gram_dve, m - 1)
                        pe.wait_ge(gram_act, m - 1)
                    for x in range(GU):
                        group = ET[:, t, GU * u + x, :, :]
                        o = psG[:, m % 2, x // GB, SF * (x % GB):SF * (x % GB + 1)]
                        last = pe.matmul(o, group.rearrange("d s f -> d (s f)"), group[:, :, 0:F], start=True, stop=True)
                    last.then_inc(multiplied, 1)

            def mlp(t):
                if t < T - 1:
                    pe.wait_ge(z_in[t], 16 * NC * S)
                else:
                    pe.wait_ge(z_in[t], 16 * (NC - 1) * S)
                    pe.wait_ge(z_last_in, 16 * S)
                if t == 0:
                    pe.wait_ge(w1_in, 16 * NC)
                    pe.wait_ge(dense_in, 32)
                else:
                    pe.wait_ge(y_ready, t)
                    pe.wait_ge(h2_act, t)
                for n in range(N1):
                    for c in range(NC):
                        last = pe.matmul(psH[:, n // 2, n % 2, :], w1_sb[0:ROWS[c], c, P * n:P * (n + 1)],
                                         zT[0:ROWS[c], t, c, :], start=c == 0, stop=c == NC - 1)
                    if n % 2 == 1:
                        last.then_inc(l1_done, 1)
                if t == 0:
                    pe.wait_ge(w2_in, 16)
                    pe.wait_ge(small_in, 48)
                pe.wait_ge(h1_dve, 2 * (t + 1))
                pe.wait_ge(h1_act, 2 * (t + 1))
                for n in range(N2):
                    for k in range(N1):
                        last = pe.matmul(psH[:, n, 2, :], w2_sb[:, k, P * n:P * (n + 1)], h1[:, k, :],
                                         start=k == 0, stop=k == N1 - 1)
                    last.then_inc(l2_done, 1)
                pe.wait_ge(h2_dve, t + 1)
                pe.wait_ge(h2_act, t + 1)
                for k in range(N2):
                    last = pe.matmul(psY, w3_sb[:, k:k + 1], h2[:, k, :], start=k == 0, stop=k == N2 - 1)
                last.then_inc(l3_done, 1)

            pe.wait_ge(ident_ready, 1)
            pe.wait_ge(pad_zero, 1)
            for n in range(FIRST):
                if fills[n][0] == "pick":
                    pick(n)
                else:
                    transposes(n)
            products(0)
            for t in range(1, T):
                for q in range(NQ):
                    transposes(FIRST + NQ * (t - 1) + q)
                products(t)
                mlp(t - 1)
            mlp(T - 1)

        @block.vector
        def _(dve):
            def ring_copy(n):
                if BY_DVE[n]:
                    dve.wait_ge(filled, n + 1)
                    dve.tensor_copy(*ring_views(n)).then_inc(et_dve, 1)

            def make_hot(k):
                if k >= 2:
                    dve.wait_ge(filled, fills.index(("pick", k - 2, None)) + 1)
                dve.tensor_copy(pick_half[:, k % 2, :], pick_ids[:, k, :]).then_inc(half_ready, 1)
                dve.wait_ge(half_ready, k + 1)
                for c in range(CH[k]):
                    no = row_no[:, int(CH[k] != min(CH)), c:c + 1]
                    last = dve.tensor_scalar(hot[:, k % 2, c, :], pick_half[:, k % 2, :], no, None, ALU.is_equal)
                last.then_inc(hot_ready, 1)

            def split_rest(k):
                whole = table[:, k % 2, 0:CH[k], :]
                dve.wait_ge(high_ready, k + 1)
                dve.tensor_tensor(whole, whole, parts[:, k % 2, 0, 0:CH[k], :], ALU.subtract).then_inc(rest_ready, 1)

            def split_low(k):
                dve.wait_ge(middle_ready, k + 1)
                dve.tensor_tensor(parts[:, k % 2, 2, 0:CH[k], :], table[:, k % 2, 0:CH[k], :],
                                  parts[:, k % 2, 1, 0:CH[k], :], ALU.subtract).then_inc(low_ready, 1)

            def gram_copies(t):
                if t >= 2:
                    dve.wait_ge(scratch_in[t - 2], 32)
                for u in range(U):
                    dve.wait_ge(multiplied, t * U + u + 1)
                    dve.tensor_copy(*gram_view(t, u, 0))
                    dve.tensor_copy(*gram_view(t, u, 1)).then_inc(gram_dve, 1)

            def relus(t):
                dve.wait_ge(l1_done, 2 * t + 1)
                for n in range(2):
                    dve.tensor_scalar(h1[:, n, :], psH[:, 0, n, :], b1_sb[:, n:n + 1], 0.0, ALU.add, ALU.max
                                      ).then_inc(h1_dve, 1)
                dve.wait_ge(l2_done, N2 * t + 1)
                dve.tensor_scalar(h2[:, 0, :], psH[:, 0, 2, :], b2_sb[:, 0:1], 0.0, ALU.add, ALU.max
                                  ).then_inc(h2_dve, 1)
                dve.wait_ge(l3_done, t + 1)
                dve.tensor_copy(y_sb[:, P * t:P * (t + 1)], psY).then_inc(y_ready, 1)

            dve.memset(ET[:, :, :, :, F:Q].rearrange("d t g s f -> d (t g s) f"), 0.0).then_inc(pad_zero, 1)
            dve.wait_ge(row_int_ready, 2)
            dve.tensor_copy(row_no[:, :, :], row_int[:, :, :]).then_inc(row_no_ready, 1)
            dve.wait_ge(row_no_ready, 1)
            dve.wait_ge(pick_ids_in, 16)
            for k in range(FP):
                make_hot(k)
                split_rest(k)
                split_low(k)
            dve.wait_ge(small_in, 48)
            gram_copies(0)
            for t in range(1, T):
                for q in range(NQ):
                    ring_copy(FIRST + NQ * (t - 1) + q)
                gram_copies(t)
                relus(t - 1)
            relus(T - 1)

        @block.scalar
        def _(act):
            def ring_copy(n):
                if not BY_DVE[n]:
                    act.wait_ge(filled, n + 1)
                    act.copy(*ring_views(n)).then_inc(et_act, 1)

            def split(k):
                whole = table[:, k % 2, 0:CH[k], :]
                act.wait_ge(table_in[k], 16)
                if k >= 2:
                    act.wait_ge(filled, fills.index(("pick", k - 2, None)) + 1)
                act.copy(parts[:, k % 2, 0, 0:CH[k], :], whole).then_inc(high_ready, 1)
                act.wait_ge(rest_ready, k + 1)
                act.copy(parts[:, k % 2, 1, 0:CH[k], :], whole).then_inc(middle_ready, 1)

            def gram_copies(t):
                if t >= 2:
                    act.wait_ge(scratch_in[t - 2], 32)
                for u in range(U):
                    act.wait_ge(multiplied, t * U + u + 1)
                    act.copy(*gram_view(t, u, 2))
                    act.copy(*gram_view(t, u, 3)).then_inc(gram_act, 1)

            def relus(t):
                act.wait_ge(l1_done, 2 * t + 2)
                for n in range(2, 4):
                    act.activation(h1[:, n, :], psH[:, 1, n - 2, :], ACT.Relu, bias=b1_sb[:, n:n + 1]
                                   ).then_inc(h1_act, 1)
                act.wait_ge(l2_done, N2 * (t + 1))
                act.activation(h2[:, 1, :], psH[:, 1, 2, :], ACT.Relu, bias=b2_sb[:, 1:2]).then_inc(h2_act, 1)

            act.dma_start(pick_ids[:, :, :], picked_ids.partition_broadcast(V)).then_inc(pick_ids_in, 16)
            split(0)
            for n in range(FIRST):
                if fills[n][0] == "pick" and fills[n][1] + 1 < FP:
                    split(fills[n][1] + 1)
                ring_copy(n)
            act.wait_ge(small_in, 48)
            gram_copies(0)
            for t in range(1, T):
                for q in range(NQ):
                    ring_copy(FIRST + NQ * (t - 1) + q)
                gram_copies(t)
                relus(t - 1)
            relus(T - 1)


def pair_rows(features, n_dense):
    n_features = len(features)
    half, each = (n_features - 1) // 2, n_features // 3
    base = n_features * (n_features - 1) // 2
    order, dense = [], 0
    for c in range(3):
        for i in range(each * c, each * (c + 1)):
            for k in range(1, half + 1):
                a, b = sorted((features[i], features[(i + k) % n_features]))
                order.append(a * n_features - a * (a + 1) // 2 + b - a - 1)
        more = min(n_dense - dense, 128 - each * half)
        order += [base + dense + x for x in range(more)]
        dense += more
    return order


PICKED = 6


def kernel(**inputs):
    import numpy as np
    import concourse.bacc as bacc
    from concourse.bass_utils import run_bass_kernel_spmd

    def columns(v):
        return np.ascontiguousarray(np.asarray(v).reshape(-1, 128).T)

    ids = np.asarray(inputs["ids"])
    by_size = sorted(range(ids.shape[1]), key=lambda f: (-inputs[f"tbl_{f}"].shape[0], f))
    gathered, picked = by_size[:-PICKED], by_size[-PICKED:]
    features = gathered + picked
    n_dense = inputs["dense_ctx"].shape[1]
    arrays = {
        "in_dense": np.ascontiguousarray(np.asarray(inputs["dense_ctx"]).T),
        "in_ids": np.ascontiguousarray(ids[:, gathered]),
        "in_picked_ids": np.ascontiguousarray(ids[:, picked].T),
        "in_w1": np.ascontiguousarray(np.asarray(inputs["W_top1"])[pair_rows(features, n_dense)]),
        "in_b1": columns(inputs["b_top1"]),
        "in_w2": np.ascontiguousarray(inputs["W_top2"]),
        "in_b2": columns(inputs["b_top2"]),
        "in_w3": columns(inputs["W_top3"]),
    }
    for f in features:
        arrays[f"in_tbl_{f}"] = np.ascontiguousarray(inputs[f"tbl_{f}"])

    nc = bacc.Bacc("TRN2", target_bir_lowering=False, num_devices=1)
    aps = {name: nc.dram_tensor(name, a.shape, mybir.dt.from_np(a.dtype), kind="ExternalInput").ap()
           for name, a in arrays.items()}
    out = nc.dram_tensor("out_y", (ids.shape[0], 1), mybir.dt.float32, kind="ExternalOutput").ap()
    dlrm_tower(nc, aps["in_dense"], aps["in_ids"], aps["in_picked_ids"],
               [aps[f"in_tbl_{f}"] for f in features], aps["in_w1"], aps["in_b1"], aps["in_w2"], aps["in_b2"], aps["in_w3"], out)
    r = run_bass_kernel_spmd(nc, [arrays], core_ids=[0])
    return r.results[0]["out_y"]
```

```python
import concourse.bass as bass
from concourse import mybir
from contextlib import ExitStack


def dlrm_tower(nc, dense_rows, ids, picked_ids, gathered_tables, picked_tables,
               w1_chunks, b1_cols, w2, b2_cols, w3_cols, out):
    fp32 = mybir.dt.float32
    fp32r = mybir.dt.float32r
    i32 = mybir.dt.int32
    ALU = mybir.AluOpType
    ACT = mybir.ActivationFunctionType

    P = 128
    B, FG = ids.shape
    FP = picked_ids.shape[0]
    F = FG + FP
    D = gathered_tables[0].shape[1]
    T = B // P
    S = 4
    G = P // S
    Q = 32
    QUADS = [list(range(f, min(f + 4, FG))) for f in range(0, FG, 4)]
    NQ = len(QUADS)
    GB = 4
    GU = 2 * GB
    U = G // GU
    J = F - 1
    W = (J - TAIL) // 2
    DN = dense_rows.shape[0]
    BLOCK_ROWS = [W * W, W * W, W * W, J * TAIL]
    ROWS = BLOCK_ROWS[:3] + [BLOCK_ROWS[3] + DN]
    NC = len(ROWS)
    N1 = w2.shape[0] // P
    N2 = w2.shape[1] // P
    ORDER = [0, 2, 1, 3]
    V = 125
    CH = [t.shape[0] // V for t in picked_tables]
    CM = max(CH)
    WARM_UP = 10
    BY_ACT = [1 if k < NQ else 2 for k in range(FP)]

    ctx = ExitStack()
    with ctx:
        def sb(name, shape, dt=fp32):
            return ctx.enter_context(nc.sbuf_tensor(name, shape, dt))

        def pb(name, shape, dt=fp32):
            return ctx.enter_context(nc.psum_tensor(name, shape, dt))

        def sem(name):
            return ctx.enter_context(nc.semaphore(name))

        ids_sb = sb("ids_sb", [P, T, FG], i32)
        pick_ids = sb("pick_ids", [V, 2, B], i32)
        row_int = sb("row_int", [V, 2, CM], i32)
        row_no = sb("row_no", [V, 2, CM])
        table = sb("table", [V, 2, CM, D])
        parts = sb("parts", [V, 2, 2, CM, D], fp32r)
        hot = sb("hot", [V, 2, CM, B], fp32r)
        ident = sb("ident", [P, P])
        rows = sb("rows", [P, 2, FG, D])
        ET = sb("ET", [P, T, G, S, Q])
        gram = sb("gram", [P, 2, J, G])
        zT = sb("zT", [P, T, NC, P])
        w1_sb = sb("w1_sb", [P, NC, N1 * P])
        w2_sb = sb("w2_sb", [P, N1, N2 * P])
        w3_sb = sb("w3_sb", [P, N2])
        b1_sb = sb("b1_sb", [P, N1])
        b2_sb = sb("b2_sb", [P, N2])
        h1 = sb("h1", [P, N1, P])
        h2 = sb("h2", [P, N2, P])
        y_sb = sb("y_sb", [1, B])

        psT = pb("psT", [P, 2, 4, P])
        psG = pb("psG", [P, 2, 2, 512])
        psH = pb("psH", [P, 2, 4, P])

        def h1_psum(t, n):
            return psG[:, n // 2, n % 2, 0:P] if t == T - 1 else psH[:, n // 2, n % 2, :]

        def h2_psum(t, n):
            return psH[:, n, 2, :] if t == T - 1 else psH[:, 0, 2 + n, :]

        def y_psum(t):
            return psH[0:1, 0 if t == T - 1 else 1, 3, :]

        psP = psG[:, :, 0, :]

        blocks = nc.dram_tensor("pair_blocks", (T, 2, P, W * G), fp32, kind="Internal").ap()
        tail = nc.dram_tensor("pair_tail", (T, P, TAIL * G), fp32, kind="Internal").ap()

        ids_in = sem("ids_in")
        ident_zero = sem("ident_zero")
        ident_ready = sem("ident_ready")
        pad_zero = sem("pad_zero")
        gram_zero = sem("gram_zero")
        w1_in = sem("w1_in")
        w2_in = sem("w2_in")
        small_in = sem("small_in")
        dense_in = sem("dense_in")
        gathered = [[sem(f"gathered_{t}_{q}") for q in range(NQ)] for t in range(T)]
        pick_ids_in = [sem(f"pick_ids_in_{k}") for k in range(FP)]
        row_int_ready = sem("row_int_ready")
        row_no_ready = sem("row_no_ready")
        table_in = [sem(f"table_in_{k}") for k in range(FP)]
        distance_ready = sem("distance_ready")
        last_hot_ready = sem("last_hot_ready")
        hot_ready = sem("hot_ready")
        high_ready = sem("high_ready")
        first_half_ready = sem("first_half_ready")
        low_ready = sem("low_ready")
        filled = sem("filled")
        picked = sem("picked")
        picked_out = sem("picked_out")
        et_dve = sem("et_dve")
        et_act = sem("et_act")
        multiplied = sem("multiplied")
        gram_dve = sem("gram_dve")
        gram_act = sem("gram_act")
        blocks_out = [[sem(f"blocks_out_{t}_{b}") for b in range(2)] for t in range(T)]
        tail_out = [sem(f"tail_out_{t}") for t in range(T)]
        chunk_in = [[sem(f"chunk_in_{t}_{c}") for c in range(NC)] for t in range(T)]
        l1_done = sem("l1_done")
        l2_done = sem("l2_done")
        l3_done = sem("l3_done")
        h1_dve = sem("h1_dve")
        h1_act = sem("h1_act")
        h2_dve = sem("h2_dve")
        h2_act = sem("h2_act")
        y_ready = sem("y_ready")
        out_done = sem("out_done")

        def row_number(k, c):
            return row_no[:, int(CH[k] != min(CH)), c:c + 1]

        BY_DVE = [n >= NQ and n % 2 == (NQ + (n // NQ == T - 1)) % 2 for n in range(T * NQ)]

        def wait_copied(eng, n):
            if sum(BY_DVE[:n]):
                eng.wait_ge(et_dve, sum(BY_DVE[:n]))
            if n - sum(BY_DVE[:n]):
                eng.wait_ge(et_act, n - sum(BY_DVE[:n]))

        def quad_views(n):
            fs = QUADS[n % NQ]
            return (ET[:, n // NQ, :, :, fs[0]:fs[-1] + 1],
                    psT[:, n % 2, 0:len(fs), :].rearrange("d f (s g) -> d g s f", s=S))

        def unit_views(m, s, banks):
            t, u = divmod(m, U)
            src = psG[Q * s:Q * s + J, m % 2, banks, 0:GB * S * J].rearrange(
                "i b (g c) -> i b g c", c=S * J)[:, :, :, J * s:J * (s + 1)]
            dst = gram[Q * s:Q * s + J, t % 2, :, GU * u:GU * (u + 1)].rearrange("i j (b g) -> i b g j", g=GB)
            return dst[:, banks], src

        UNIT_BANKS = [[slice(0, 2)]] * (T * U - 1) + [[slice(0, 1), slice(1, 2)]]

        steps = []
        units = [("unit", m) for m in range(T * U)]
        quads = [("quad", n) for n in range(T * NQ)]
        for t in range(T - 1):
            un, qu = units[U * t:U * (t + 1)], quads[NQ * (t + 1):NQ * (t + 2)]
            if t == 0:
                steps += [qu[0], un[0], qu[1], un[1], qu[2], un[2]] + qu[3:] + [un[3]]
            else:
                steps += [un[0]] + ([("layer3", t - 2)] if t >= 2 else [])
                steps += [un[1], qu[0], un[2], qu[1], un[3], qu[2]]
                mlp = [("layer1", t - 1), ("layer2", t - 1), ("layer2_end", t - 1)]
                if t < T - 2:
                    steps += [mlp[0], qu[3], mlp[1], qu[4], mlp[2]]
                else:
                    steps += [mlp[0], qu[3], mlp[1], mlp[2], qu[4]]
        steps += [("layer3", T - 3)] + units[U * (T - 1):]
        steps += [("layer1", T - 2), ("layer2", T - 2), ("layer2_end", T - 2),
                  ("chunk", 0), ("chunk", 1), ("layer3", T - 2), ("chunk", 2), ("chunk", 3),
                  ("relu1", T - 1), ("layer2", T - 1), ("layer3", T - 1)]

        block = ctx.enter_context(nc.Block())

        @block.sync
        def _(sp):
            sp.dma_start(ids_sb[:, :, :], ids.rearrange("(t p) f -> p t f", p=P)).then_inc(ids_in, 16)
            for k in range(FP):
                if k >= 2:
                    sp.wait_ge(hot_ready, sum(CH[:k - 1]) - sum(BY_ACT[:k - 1]))
                    sp.wait_ge(last_hot_ready, sum(BY_ACT[:k - 1]))
                if k >= 1:
                    sp.dma_start(pick_ids[:, k % 2, :], picked_ids[k].partition_broadcast(V)
                                 ).then_inc(pick_ids_in[k], 16)
                if k >= 2:
                    sp.wait_ge(low_ready, k - 1)
                sp.dma_start(table[:, k % 2, 0:CH[k], :],
                             picked_tables[k].rearrange("(p c) d -> p c d", c=CH[k])).then_inc(table_in[k], 16)
            sp.dma_start(w1_sb[:, :, :], w1_chunks).then_inc(w1_in, 16)
            sp.dma_start(zT[BLOCK_ROWS[3]:ROWS[3], :, 3, :],
                         dense_rows.rearrange("k (t p) -> k t p", p=P)).then_inc(dense_in, 16)
            sp.dma_start(w2_sb[:, :, :], w2.rearrange("(k p) n -> p k n", p=P)).then_inc(w2_in, 16)
            sp.dma_start(b1_sb[:, :], b1_cols).then_inc(small_in, 16)
            sp.dma_start(b2_sb[:, :], b2_cols).then_inc(small_in, 16)
            sp.dma_start(w3_sb[:, :], w3_cols).then_inc(small_in, 16)

            def read_rows(t, c, block, i0, ni, w):
                src = block.rearrange("(s i) (j g) -> s i j g", s=S, g=G)[:, i0:i0 + ni, :, :].rearrange(
                    "s i j g -> (i j) s g")
                sp.dma_start(zT[0:ni * w, t, c, :].rearrange("r (s g) -> r s g", s=S), src
                             ).then_inc(chunk_in[t][c], 16)

            for t in range(T):
                sp.wait_ge(gram_dve, U * (t + 1))
                sp.wait_ge(gram_act, U * (t + 1))
                for b in range(2):
                    sp.dma_start(blocks[t, b], gram[:, t % 2, W * b:W * (b + 1), :].rearrange("p j g -> p (j g)")
                                 ).then_inc(blocks_out[t][b], 16)
                sp.dma_start(tail[t], gram[:, t % 2, 2 * W:J, :].rearrange("p j g -> p (j g)")
                             ).then_inc(tail_out[t], 16)
                sp.wait_ge(blocks_out[t][0], 16)
                read_rows(t, 0, blocks[t, 0], 0, W, W)
                sp.wait_ge(blocks_out[t][1], 16)
                read_rows(t, 1, blocks[t, 1], 0, W, W)
                read_rows(t, 2, blocks[t, 1], W, W, W)
                sp.wait_ge(tail_out[t], 16)
                read_rows(t, 3, tail[t], 0, J, TAIL)
            sp.wait_ge(y_ready, T)
            sp.dma_start(out.rearrange("b o -> o b"), y_sb[:, :]).then_inc(out_done, 16)
            sp.wait_ge(out_done, 16)

        @block.gpsimd
        def _(pool):
            pool.memset(ident[:, :], 0.0).then_inc(ident_zero, 1)
            pool.wait_ge(ident_zero, 1)
            pool.affine_select(out=ident[:, :], in_=ident[:, :], compare_op=ALU.not_equal, fill=1.0, base=0,
                               pattern=[[-1, P]], channel_multiplier=1).then_inc(ident_ready, 1)
            for x, chunks in enumerate((min(CH), max(CH))):
                pool.iota(row_int[:, x, :], pattern=[[1, CM]], base=0, channel_multiplier=chunks
                          ).then_inc(row_int_ready, 1)
            pool.wait_ge(ids_in, 16)
            for t in range(T):
                if t >= 2:
                    pool.wait_ge(filled, NQ * (t - 1))
                for q in range(NQ):
                    for f in QUADS[q]:
                        pool.indirect_dma_start(
                            out=rows[:, t % 2, f, :], out_offset=None, in_=gathered_tables[f],
                            in_offset=bass.IndirectOffsetOnAxis(ap=ids_sb[:, t, f:f + 1], axis=0),
                        ).then_inc(gathered[t][q], 16)

        @block.tensor
        def _(pe):
            def transposes(n):
                t, q = divmod(n, NQ)
                pe.wait_ge(gathered[t][q], 16 * len(QUADS[q]))
                if n >= 2:
                    wait_copied(pe, n - 1)
                for x, f in enumerate(QUADS[q]):
                    last = pe.transpose(psT[:, n % 2, x, :], rows[:, t % 2, f, :], ident[:, :])
                last.then_inc(filled, 1)

            def pick(k):
                if k >= 2:
                    pe.wait_ge(picked_out, k - 1)
                for x, ready in enumerate((high_ready, low_ready)):
                    if k == 0 and x == 0:
                        pe.wait_ge(first_half_ready, 1)
                    else:
                        pe.wait_ge(ready, k + 1)
                    for c in range(CH[k]):
                        if k == 0 and x == 0 and c == CH[k] // 2:
                            pe.wait_ge(high_ready, 1)
                        if x == 0:
                            own = CH[k] - BY_ACT[k]
                            if c < own:
                                pe.wait_ge(hot_ready, sum(CH[:k]) - sum(BY_ACT[:k]) + c + 1)
                            else:
                                pe.wait_ge(last_hot_ready, sum(BY_ACT[:k]) + c - own + 1)
                        last = pe.matmul(psP[:, k % 2, :], parts[:, k % 2, x, c, :], hot[:, k % 2, c, :],
                                         start=x == 0 and c == 0, stop=x == 1 and c == CH[k] - 1)
                last.then_inc(picked, 1)

            def product_unit(m):
                t, u = divmod(m, U)
                if u == 0:
                    wait_copied(pe, NQ * (t + 1))
                if m == 0:
                    pe.wait_ge(picked_out, FP)
                if m >= 2:
                    pe.wait_ge(gram_dve, m - 1)
                    pe.wait_ge(gram_act, m - 1)
                for x in range(GU):
                    group = ET[:, t, GU * u + x, :, :]
                    stationary = group.rearrange("d s f -> d (s f)")[:, 0:Q * (S - 1) + J]
                    o = psG[0:Q * (S - 1) + J, m % 2, x // GB, S * J * (x % GB):S * J * (x % GB + 1)]
                    last = pe.matmul(o, stationary, group[:, :, 1:F], start=True, stop=True)
                    if x + 1 in [GB * banks.stop for banks in UNIT_BANKS[m]]:
                        last.then_inc(multiplied, 1)

            def layer1(t):
                for c in range(NC):
                    pe.wait_ge(chunk_in[t][c], 16)
                if t == 0:
                    pe.wait_ge(w1_in, 16)
                    pe.wait_ge(dense_in, 16)
                else:
                    pe.wait_ge(y_ready, t)
                for n in range(N1):
                    for c in range(NC):
                        last = pe.matmul(psH[:, n // 2, n % 2, :], w1_sb[0:ROWS[c], c, P * n:P * (n + 1)],
                                         zT[0:ROWS[c], t, c, :], start=c == 0, stop=c == NC - 1)
                    if n % 2 == 1:
                        last.then_inc(l1_done, 1)

            def last_layer1(c):
                if c == 0:
                    pe.wait_ge(gram_dve, U * T)
                    pe.wait_ge(gram_act, U * T)
                pe.wait_ge(chunk_in[T - 1][c], 16)
                for n in ORDER:
                    last = pe.matmul(psG[:, n // 2, n % 2, 0:P], w1_sb[0:ROWS[c], c, P * n:P * (n + 1)],
                                     zT[0:ROWS[c], T - 1, c, :], start=c == 0, stop=c == NC - 1)
                    if c == NC - 1:
                        last.then_inc(l1_done, 1)

            def layer2(t, outputs):
                if t == 0:
                    pe.wait_ge(w2_in, 16)
                if t < T - 1:
                    pe.wait_ge(h1_dve, 2 * (t + 1))
                if t < T - 1:
                    order = [(k, n) for n in outputs for k in range(N1)]
                else:
                    order = [(k, n) for n in outputs for k in ORDER]
                first, end = order[0][0], order[-1][0]
                for k, n in order:
                    pe.wait_ge(h1_dve if k < 2 else h1_act, 2 * t + 1 + k % 2)
                    last = pe.matmul(h2_psum(t, n), w2_sb[:, k, P * n:P * (n + 1)], h1[:, k, :],
                                     start=k == first, stop=k == end)
                    if k == end:
                        last.then_inc(l2_done, 1)

            def layer3(t):
                if t == 0:
                    pe.wait_ge(small_in, 48)
                for k in range(N2):
                    if k == 1 and t == T - 1:
                        pe.wait_ge(h2_act, 1)
                    else:
                        pe.wait_ge(h2_dve, N2 * t + k + 1)
                    last = pe.matmul(y_psum(t), w3_sb[:, k:k + 1], h2[:, k, :], start=k == 0, stop=k == N2 - 1)
                last.then_inc(l3_done, 1)

            pe.wait_ge(ident_ready, 1)
            for x in range(WARM_UP):
                pe.matmul(psH[:, 0, 0, :], ident[:, :], ident[:, :], start=True, stop=True)
            for x in range(max(FP, NQ)):
                if x < FP:
                    pick(x)
                if x < NQ:
                    transposes(x)
            pe.wait_ge(pad_zero, T)
            for step, x in steps:
                if step == "unit":
                    product_unit(x)
                elif step == "quad":
                    transposes(x)
                elif step == "layer1":
                    layer1(x)
                elif step == "layer2":
                    layer2(x, range(1 if x < T - 1 else N2))
                elif step == "layer2_end":
                    layer2(x, range(1, N2))
                elif step == "layer3":
                    layer3(x)
                elif step == "chunk":
                    last_layer1(x)

        @block.vector
        def _(dve):
            def quad_copy(n):
                if BY_DVE[n]:
                    dve.wait_ge(filled, n + 1)
                    dve.tensor_copy(*quad_views(n)).then_inc(et_dve, 1)

            def make_hot(k):
                dve.wait_ge(pick_ids_in[k], 16)
                if k >= 2:
                    dve.wait_ge(picked, k - 1)
                for c in range(CH[k] - BY_ACT[k]):
                    dve.tensor_scalar(hot[:, k % 2, c, :], pick_ids[:, k % 2, :], row_number(k, c), None, ALU.is_equal
                                      ).then_inc(hot_ready, 1)

            def split_low(k):
                dve.wait_ge(high_ready, k + 1)
                dve.tensor_tensor(parts[:, k % 2, 1, 0:CH[k], :], table[:, k % 2, 0:CH[k], :],
                                  parts[:, k % 2, 0, 0:CH[k], :], ALU.subtract).then_inc(low_ready, 1)

            def unit_copies(m):
                if m // U >= 2:
                    dve.wait_ge(blocks_out[m // U - 2][0], 16)
                    dve.wait_ge(blocks_out[m // U - 2][1], 16)
                    dve.wait_ge(tail_out[m // U - 2], 16)
                for x, banks in enumerate(UNIT_BANKS[m]):
                    dve.wait_ge(multiplied, m + x + 1)
                    dve.tensor_copy(*unit_views(m, 0, banks))
                    last = dve.tensor_copy(*unit_views(m, 1, banks))
                last.then_inc(gram_dve, 1)

            def relu1(t):
                for n in range(2):
                    dve.wait_ge(l1_done, 2 * t + 1 + (2 * n if t == T - 1 else 0))
                    dve.tensor_scalar(h1[:, n, :], h1_psum(t, n), b1_sb[:, n:n + 1], 0.0, ALU.add, ALU.max
                                      ).then_inc(h1_dve, 1)

            def relu2(t):
                if t < T - 1:
                    dve.wait_ge(l2_done, N2 * (t + 1))
                else:
                    dve.wait_ge(l2_done, N2 * t + 1)
                for n in range(N2 if t < T - 1 else 1):
                    dve.tensor_scalar(h2[:, n, :], h2_psum(t, n), b2_sb[:, n:n + 1], 0.0, ALU.add, ALU.max
                                      ).then_inc(h2_dve, 1)

            def take_y(t):
                dve.wait_ge(l3_done, t + 1)
                dve.tensor_copy(y_sb[:, P * t:P * (t + 1)], y_psum(t)).then_inc(y_ready, 1)

            dve.memset(gram[:, :, :, :].rearrange("p b j g -> p (b j g)"), 0.0).then_inc(gram_zero, 1)
            dve.wait_ge(row_no_ready, 1)
            for k in range(FP):
                make_hot(k)
                split_low(k)
            dve.wait_ge(small_in, 48)
            for step, x in steps:
                if step == "unit":
                    unit_copies(x)
                elif step == "quad":
                    quad_copy(x)
                elif step in ("layer1", "relu1"):
                    relu1(x)
                elif step == "layer2_end" or step == "layer2" and x == T - 1:
                    relu2(x)
                elif step == "layer3":
                    take_y(x)

        @block.scalar
        def _(act):
            def quad_copy(n):
                if not BY_DVE[n]:
                    act.wait_ge(filled, n + 1)
                    act.copy(*quad_views(n)).then_inc(et_act, 1)

            def pick_copy(k):
                act.wait_ge(picked, k + 1)
                act.copy(ET[:, :, :, :, FG + k], psP[:, k % 2, :].rearrange("d (t s g) -> d t g s", t=T, s=S)
                         ).then_inc(picked_out, 1)

            def split_high(k):
                act.wait_ge(table_in[k], 16)
                if k >= 2:
                    act.wait_ge(picked, k - 1)
                half = CH[k] // 2
                if k == 0:
                    act.copy(parts[:, k % 2, 0, 0:half, :], table[:, k % 2, 0:half, :]).then_inc(first_half_ready, 1)
                    act.copy(parts[:, k % 2, 0, half:CH[k], :], table[:, k % 2, half:CH[k], :]).then_inc(high_ready, 1)
                else:
                    act.copy(parts[:, k % 2, 0, 0:CH[k], :], table[:, k % 2, 0:CH[k], :]).then_inc(high_ready, 1)

            def make_last_hot(k):
                act.wait_ge(pick_ids_in[k], 16)
                chunks = range(CH[k] - BY_ACT[k], CH[k])
                for c in chunks:
                    act.activation(hot[:, k % 2, c, :], pick_ids[:, k % 2, :], ACT.Abs, bias=row_number(k, c),
                                   scale=-1.0).then_inc(distance_ready, 1)
                for x, c in enumerate(chunks):
                    act.wait_ge(distance_ready, sum(BY_ACT[:k]) + x + 1)
                    act.activation(hot[:, k % 2, c, :], hot[:, k % 2, c, :], ACT.Relu, bias=1.0, scale=-1.0
                                   ).then_inc(last_hot_ready, 1)

            def zero_pads(t):
                act.wait_ge(gram_zero, 1)
                act.copy(ET[:, t, :, :, F:Q].rearrange("d g s f -> d (g s) f"),
                         gram[:, 0, 0:S * (Q - F), :].rearrange("d f g -> d (f g)").rearrange(
                             "d (x f) -> d x f", f=Q - F)).then_inc(pad_zero, 1)

            def unit_copies(m):
                if m // U >= 2:
                    act.wait_ge(blocks_out[m // U - 2][0], 16)
                    act.wait_ge(blocks_out[m // U - 2][1], 16)
                    act.wait_ge(tail_out[m // U - 2], 16)
                for x, banks in enumerate(UNIT_BANKS[m]):
                    act.wait_ge(multiplied, m + x + 1)
                    act.copy(*unit_views(m, 2, banks))
                    last = act.copy(*unit_views(m, 3, banks))
                last.then_inc(gram_act, 1)

            def relu1(t):
                for n in range(2, 4):
                    act.wait_ge(l1_done, 2 * t + 2 + (2 * (n - 2) if t == T - 1 else 0))
                    act.activation(h1[:, n, :], h1_psum(t, n), ACT.Relu, bias=b1_sb[:, n:n + 1]).then_inc(h1_act, 1)

            def last_relu2():
                act.wait_ge(l2_done, N2 * T)
                act.activation(h2[:, 1, :], h2_psum(T - 1, 1), ACT.Relu, bias=b2_sb[:, 1:2]).then_inc(h2_act, 1)

            act.dma_start(pick_ids[:, 0, :], picked_ids[0].partition_broadcast(V)).then_inc(pick_ids_in[0], 16)
            act.wait_ge(row_int_ready, 2)
            act.copy(row_no[:, :, :], row_int[:, :, :]).then_inc(row_no_ready, 1)
            act.wait_ge(row_no_ready, 1)
            split_high(0)
            make_last_hot(0)
            for x in range(max(FP, NQ)):
                if x + 1 < FP:
                    split_high(x + 1)
                    make_last_hot(x + 1)
                if x < FP:
                    pick_copy(x)
                if x < NQ:
                    quad_copy(x)
                if x < T:
                    zero_pads(x)
            act.wait_ge(small_in, 48)
            act.wait_ge(gram_zero, 1)
            for step, x in steps:
                if step == "unit":
                    unit_copies(x)
                elif step == "quad":
                    quad_copy(x)
                elif step in ("layer1", "relu1"):
                    relu1(x)
                elif step == "layer2" and x == T - 1:
                    last_relu2()


def feature_order(sizes, picked):
    by_size = sorted(range(len(sizes)), key=lambda f: (-sizes[f], f))
    gather, pick = by_size[:-picked], by_size[-picked:]
    return gather, pick[::-1]


def chunk_rows(features, n_dense):
    n = len(features)
    w = (n - 1 - TAIL) // 2

    def pair(i, j):
        a, b = sorted((features[i], features[j]))
        return a * n - a * (a + 1) // 2 + b - a - 1 if i < j else -1

    chunks = [[pair(i, j) for i in range(w) for j in range(1, w + 1)],
              [pair(i, j) for i in range(w) for j in range(w + 1, 2 * w + 1)],
              [pair(i, j) for i in range(w, 2 * w) for j in range(w + 1, 2 * w + 1)],
              [pair(i, j) for i in range(n - 1) for j in range(n - TAIL, n)]]
    chunks[3] += [n * (n - 1) // 2 + x for x in range(n_dense)]
    return [c + [-1] * (128 - len(c)) for c in chunks]


PICKED = 9
TAIL = 4


def kernel(**inputs):
    import numpy as np
    import concourse.bacc as bacc
    from concourse.bass_utils import run_bass_kernel_spmd

    def columns(v):
        return np.ascontiguousarray(np.asarray(v).reshape(-1, 128).T)

    ids = np.asarray(inputs["ids"])
    n_dense = inputs["dense_ctx"].shape[1]
    gather, pick = feature_order([inputs[f"tbl_{f}"].shape[0] for f in range(ids.shape[1])], PICKED)

    w1 = np.asarray(inputs["W_top1"])
    w1_chunks = np.zeros((128, 4, w1.shape[1]), w1.dtype)
    for c, chunk in enumerate(chunk_rows(gather + pick, n_dense)):
        for p, row in enumerate(chunk):
            if row >= 0:
                w1_chunks[p, c] = w1[row]

    arrays = {
        "in_dense": np.ascontiguousarray(np.asarray(inputs["dense_ctx"]).T),
        "in_ids": np.ascontiguousarray(ids[:, gather]),
        "in_picked_ids": np.ascontiguousarray(ids[:, pick].T),
        "in_w1": w1_chunks,
        "in_b1": columns(inputs["b_top1"]),
        "in_w2": np.ascontiguousarray(inputs["W_top2"]),
        "in_b2": columns(inputs["b_top2"]),
        "in_w3": columns(inputs["W_top3"]),
    }
    for f in gather + pick:
        arrays[f"in_tbl_{f}"] = np.ascontiguousarray(inputs[f"tbl_{f}"])

    nc = bacc.Bacc("TRN2", target_bir_lowering=False, num_devices=1)
    aps = {name: nc.dram_tensor(name, a.shape, mybir.dt.from_np(a.dtype), kind="ExternalInput").ap()
           for name, a in arrays.items()}
    out = nc.dram_tensor("out_y", (ids.shape[0], 1), mybir.dt.float32, kind="ExternalOutput").ap()
    dlrm_tower(nc, aps["in_dense"], aps["in_ids"], aps["in_picked_ids"],
               [aps[f"in_tbl_{f}"] for f in gather], [aps[f"in_tbl_{f}"] for f in pick],
               aps["in_w1"], aps["in_b1"], aps["in_w2"], aps["in_b2"], aps["in_w3"], out)
    r = run_bass_kernel_spmd(nc, [arrays], core_ids=[0])
    return r.results[0]["out_y"]
```
